# Optimizing a Trainium2 kernel written in Bass

```python
import numpy as np
import jax
import jax.numpy as jnp

def _softmax(x, axis=-1):
    return jax.nn.softmax(x, axis=axis)

def _gelu(x):
    return jax.nn.gelu(x, approximate=True)

def _silu(x):
    return jax.nn.silu(x)

def _sigmoid(x):
    return jax.nn.sigmoid(x)

def _layernorm(x, axis=-1, eps=1e-05):
    m = jnp.mean(x, axis=axis, keepdims=True)
    v = jnp.var(x, axis=axis, keepdims=True)
    return (x - m) / jnp.sqrt(v + eps)

def _scatter_add(tgt, idx, src, axis=0):
    return tgt.at[idx].add(src)

def _segment_sum(src, seg, n):
    return jax.ops.segment_sum(src, seg, n)
kernel_name = 'mk_flamingo_gated_d1_seqx_r2_450820'

def setup_inputs(seed: int=0):
    np.random.seed(seed)
    _w = jnp.asarray

    def _rec_inputs():
        import jax
        import jax.numpy as jnp
        _rk = jax.random.key(seed)
        x = 7.22e-05 + 1 * jax.random.normal(jax.random.fold_in(_rk, 1), (16, 512, 1024), jnp.float32)
        _lenS = 512 - jax.random.randint(jax.random.fold_in(_rk, 7), (16,), 0, max(1, 512 // 4) + 1, jnp.int32)
        _lenS2 = 512 - jax.random.randint(jax.random.fold_in(_rk, 8), (16,), 0, max(1, 512 // 4) + 1, jnp.int32)
        _ctx_2048P = jax.random.normal(jax.random.fold_in(_rk, 11), (16, 16, 1024), jnp.float32)
        _ctx_2048c = jax.random.dirichlet(jax.random.fold_in(_rk, 511), 0.3 * jnp.ones((16,), jnp.float32), (16, 512))
        _ctx_2048t = jnp.einsum('bsk,bkd->bsd', _ctx_2048c, _ctx_2048P)
        _ctx_2048t = _ctx_2048t * jax.lax.rsqrt(jnp.mean(jnp.square(_ctx_2048t)) + 1e-12) * 0.953939
        ctx_2048 = 4.13588e-05 + 0.999923 * (_ctx_2048t + 0.3 * jax.random.normal(jax.random.fold_in(_rk, 611), (16, 512, 1024), jnp.float32))
        _g = jax.random.normal(jax.random.fold_in(_rk, 9001), (2, 1), jnp.float32)
        _g = jnp.sign(_g) * jnp.maximum(jnp.abs(_g), 1.0) + (_g == 0) * 1.0
        g_xattn = _g[0]
        g_ffn = _g[1]
        return (x, ctx_2048, g_xattn, g_ffn)
    x, ctx_2048, g_xattn, g_ffn = _rec_inputs()

    def _L0_xattn_setup():
        import jax, jax.numpy as jnp
        import numpy as np
        B, D, N, H = (4, 512, 1024, 16)
        HD = D // H

        def rotate_half(x):
            x1 = x[..., 0::2]
            x2 = x[..., 1::2]
            return jnp.stack((-x2, x1), axis=-1).reshape(x.shape)

        def apply_cached_rotary_emb(freqs, t):
            return t * freqs[0] + rotate_half(t) * freqs[1]
        key = jax.random.key(seed)
        ks = jax.random.split(key, 13)
        s = 1.0 / np.sqrt(D)
        inp = {'query': jax.random.normal(ks[0], (B, D, N), jnp.float32), 'key': jax.random.normal(ks[1], (B, D, N), jnp.float32), 'value': jax.random.normal(ks[2], (B, D, N), jnp.float32), 'encoding': jax.random.normal(ks[3], (2, 1, 1, N, HD), jnp.float32), 'Wq': jax.random.normal(ks[4], (D, D), jnp.float32) * s, 'bq': jax.random.normal(ks[5], (D,), jnp.float32) * s, 'Wk': jax.random.normal(ks[6], (D, D), jnp.float32) * s, 'bk': jax.random.normal(ks[7], (D,), jnp.float32) * s, 'Wv': jax.random.normal(ks[8], (D, D), jnp.float32) * s, 'bv': jax.random.normal(ks[9], (D,), jnp.float32) * s, 'Wm': jax.random.normal(ks[10], (D, D), jnp.float32) * s, 'bm': jax.random.normal(ks[11], (D,), jnp.float32) * s}
        return inp
    _L0_xattn_all = _L0_xattn_setup()
    _L0_xattn_in = {k: v for k, v in _L0_xattn_all.items() if k in ('encoding', 'Wq', 'bq', 'Wk', 'bk', 'Wv', 'bv', 'Wm', 'bm')}
    del _L0_xattn_all

    def _L0_ffn_setup():
        import jax, jax.numpy as jnp
        import numpy as np
        TOP_K = 2
        key = jax.random.key(seed)
        ks = jax.random.split(key, 4)
        G, S, F, E, H = (4, 1024, 1024, 8, 1024)
        return {'x': jax.random.normal(ks[0], (G, S, F), dtype=jnp.float32), 'router_logits': jax.random.normal(ks[1], (F, E), dtype=jnp.float32) * 0.02, 'gating_einsum': jax.random.normal(ks[2], (E, 2, H, F), dtype=jnp.float32) * 0.02, 'linear': jax.random.normal(ks[3], (E, H, F), dtype=jnp.float32) * 0.02, 'per_expert_scale': jnp.ones((E,), dtype=jnp.float32), 'router_scale': jnp.ones((F,), dtype=jnp.float32)}
    _L0_ffn_all = _L0_ffn_setup()
    _L0_ffn_in = {k: v for k, v in _L0_ffn_all.items() if k in ('router_logits', 'gating_einsum', 'linear', 'per_expert_scale', 'router_scale')}
    del _L0_ffn_all
    return {'x': x, 'ctx_2048': ctx_2048, 'g_xattn': g_xattn, 'g_ffn': g_ffn, 'L0_xattn_encoding': _L0_xattn_in['encoding'], 'L0_xattn_Wq': _L0_xattn_in['Wq'], 'L0_xattn_bq': _L0_xattn_in['bq'], 'L0_xattn_Wk': _L0_xattn_in['Wk'], 'L0_xattn_bk': _L0_xattn_in['bk'], 'L0_xattn_Wv': _L0_xattn_in['Wv'], 'L0_xattn_bv': _L0_xattn_in['bv'], 'L0_xattn_Wm': _L0_xattn_in['Wm'], 'L0_xattn_bm': _L0_xattn_in['bm'], 'L0_ffn_router_logits': _L0_ffn_in['router_logits'], 'L0_ffn_gating_einsum': _L0_ffn_in['gating_einsum'], 'L0_ffn_linear': _L0_ffn_in['linear'], 'L0_ffn_per_expert_scale': _L0_ffn_in['per_expert_scale'], 'L0_ffn_router_scale': _L0_ffn_in['router_scale']}

def reference(x, ctx_2048, g_xattn, g_ffn, L0_xattn_encoding, L0_xattn_Wq, L0_xattn_bq, L0_xattn_Wk, L0_xattn_bk, L0_xattn_Wv, L0_xattn_bv, L0_xattn_Wm, L0_xattn_bm, L0_ffn_router_logits, L0_ffn_gating_einsum, L0_ffn_linear, L0_ffn_per_expert_scale, L0_ffn_router_scale):
    import jax
    import jax.numpy as jnp

    def _L0_xattn_ref(query, key, value, encoding, Wq, bq, Wk, bk, Wv, bv, Wm, bm):
        import jax, jax.numpy as jnp
        import numpy as np
        B, D, N, H = (4, 512, 1024, 16)
        HD = D // H

        def rotate_half(x):
            x1 = x[..., 0::2]
            x2 = x[..., 1::2]
            return jnp.stack((-x2, x1), axis=-1).reshape(x.shape)

        def apply_cached_rotary_emb(freqs, t):
            return t * freqs[0] + rotate_half(t) * freqs[1]
        b, d_model, n = query.shape

        def proj(W, bias, x):
            return jnp.einsum('oi,bin->bon', W, x) + bias[None, :, None]
        q = proj(Wq, bq, query).reshape(b, HD, H, n)
        k = proj(Wk, bk, key).reshape(b, HD, H, n)
        v = proj(Wv, bv, value).reshape(b, HD, H, n)
        q = jnp.transpose(apply_cached_rotary_emb(encoding, jnp.transpose(q, (0, 2, 3, 1))), (0, 3, 1, 2))
        k = jnp.transpose(apply_cached_rotary_emb(encoding, jnp.transpose(k, (0, 2, 3, 1))), (0, 3, 1, 2))
        scores = jnp.einsum('bdhn,bdhm->bhnm', q, k) / np.float32(np.sqrt(HD))
        prob = jax.nn.softmax(scores, axis=-1)
        x = jnp.einsum('bhnm,bdhm->bdhn', prob, v)
        out = jnp.einsum('oi,bin->bon', Wm, x.reshape(b, d_model, n)) + bm[None, :, None]
        return out

    def _L0_ffn_ref(x, router_logits, gating_einsum, linear, per_expert_scale, router_scale):
        import jax, jax.numpy as jnp
        import numpy as np
        TOP_K = 2
        G, S, F = x.shape
        E = router_logits.shape[-1]
        H = linear.shape[1]
        k = TOP_K
        dtype = x.dtype
        var = jnp.mean(jnp.square(x.astype(jnp.float32)), axis=-1, keepdims=True)
        router_input = x * jax.lax.rsqrt(var + 1e-06).astype(dtype)
        root_size = jax.lax.rsqrt(jnp.array(F, dtype=dtype))
        router_input = router_input * root_size * router_scale.astype(dtype)
        logits = jnp.einsum('gsd,de->gse', router_input, router_logits.astype(dtype))
        logits32 = logits.astype(jnp.float32)
        probs = jax.nn.softmax(logits32, axis=-1)
        _, choices = jax.lax.approx_max_k(logits32, k=k)
        indicator = jax.nn.one_hot(choices, E, dtype=probs.dtype).sum(axis=-2)
        renorm = jnp.sum(indicator * probs, axis=-1, keepdims=True)
        renorm = jnp.where(renorm > 0.0, renorm, 1.0)
        weights = probs / renorm
        x_flat = x.reshape((-1, F))
        batch_size = G * S
        choices_flat = choices.ravel()
        xs_order = choices_flat.argsort()
        xs_reverse_argsort = xs_order.argsort()
        xs_indices = jnp.repeat(jnp.arange(batch_size), k)[xs_order]
        sorted_xs = x_flat[xs_indices, :]
        choices_oh = jax.nn.one_hot(choices, num_classes=E, dtype=jnp.int32)
        tokens_per_expert = jnp.sum(choices_oh, axis=(0, 1, 2))
        combine_weights = (choices_oh.astype(jnp.float32) * jnp.expand_dims(weights, axis=2)).sum(axis=-1).astype(weights.dtype)
        w_gate = jnp.transpose(gating_einsum, (0, 3, 1, 2)).reshape(E, F, 2 * H)
        gate_out = jax.lax.ragged_dot(sorted_xs, w_gate.astype(dtype), group_sizes=tokens_per_expert)
        gate_out = gate_out.reshape(gate_out.shape[0], 2, H)
        activation = jax.nn.gelu(gate_out[:, 0, :]) * gate_out[:, 1, :]
        expert_outputs = jax.lax.ragged_dot(activation, linear.astype(dtype), group_sizes=tokens_per_expert)
        expert_indices = jnp.repeat(jnp.arange(E), tokens_per_expert, total_repeat_length=expert_outputs.shape[0])
        expert_outputs = expert_outputs * per_expert_scale.astype(expert_outputs.dtype)[expert_indices, None]
        out = expert_outputs[xs_reverse_argsort].reshape((G, S, k, -1))
        out = jnp.einsum('blkd,blk->bld', out, combine_weights, preferred_element_type=out.dtype)
        return out
    x = x + jnp.tanh(g_xattn[0]) * _L0_xattn_ref(_layernorm(x, axis=-1), ctx_2048, ctx_2048, L0_xattn_encoding, L0_xattn_Wq, L0_xattn_bq, L0_xattn_Wk, L0_xattn_bk, L0_xattn_Wv, L0_xattn_bv, L0_xattn_Wm, L0_xattn_bm)
    x = x + jnp.tanh(g_ffn[0]) * _L0_ffn_ref(_layernorm(x, axis=-1), L0_ffn_router_logits, L0_ffn_gating_einsum, L0_ffn_linear, L0_ffn_per_expert_scale, L0_ffn_router_scale)
    return x

_drawn_inputs = setup_inputs


def setup_inputs(seed=0):
    import zlib

    import numpy as np

    out = dict(_drawn_inputs(seed))
    spreads = {'L0_ffn_per_expert_scale': (1.0, 0.6), 'L0_ffn_router_scale': (1.0, 0.2)}
    factors = {}
    for name, (base, spread) in spreads.items():
        noise = np.random.default_rng([zlib.crc32(name.encode()), seed]).standard_normal(out[name].shape)
        drawn = base * np.exp(spread * noise) if base else spread * noise
        out[name] = jnp.asarray(drawn.astype(out[name].dtype))
    for name, factor in factors.items():
        out[name] = (out[name] * factor).astype(out[name].dtype)
    return out
```

```python
from contextlib import ExitStack

import concourse.bass as bass
from concourse import mybir

F32 = mybir.dt.float32
F16 = mybir.dt.float16
I32 = mybir.dt.int32
U32 = mybir.dt.uint32
ACT = mybir.ActivationFunctionType
ALU = mybir.AluOpType
AX = mybir.AxisListType

P = 128
HALF = 512
S_ACT = 16.0
S_E = 256.0
S_W = 256.0
LN_EPS = 1e-5
HD = 32


def attention_phase(nc, keep, dram, shapes):
    B, N, H, F = shapes["B"], shapes["N"], shapes["H"], shapes["F"]
    C = H * HD
    KC = C // P
    G = C // P
    HG = P // HD
    NT = N // P
    FC = N // P
    E = shapes["E"]
    UNITS = HG * NT
    LEAD = 8
    EW = F // 2
    CB = shapes["CHUNKS"] * 2 // B
    assert CB * B == shapes["CHUNKS"] * 2 and CB == 24 and NT == 8 and G == 4
    inv_ps = 1.0 / (S_ACT * S_W)

    def rope_steps(r, g, at):
        yield at, ("qk", r, g)
        for i, (swap, add) in enumerate(((3, 8), (12, 17))):
            for half in range(2):
                yield at + swap + half, ("swap", r, g, i, half)
                yield at + add + half, ("sum", r, g, i, half)
            yield at + add + 2, ("hi", r, g, i)

    def group_slots(g, first, last):
        slots = [[] for _ in range(UNITS)]
        r, ahead = (0, g + 2) if g + 2 < G else (1, g + 2 - G)
        begin = 4 if g in (0, 2) else 0
        if not (last and r == 1):
            for at, step in rope_steps(r, ahead, begin):
                slots[at].append(step)
        if g >= 1:
            slots[4 if begin else 3].append(("den", 0, g - 1))
            scales, out = ((10, 11), 15) if last and r == 1 else ((5, 6), 10) if begin else ((7, 11), 14)
            for half in range(2):
                slots[scales[half]].append(("scale", 0, g - 1, half))
            slots[out].append(("out", 0, g - 1))
            r, ahead = (0, g + 1) if g + 1 < G else (1, g + 1 - G)
            if not (last and r == 1):
                for h in range(HG):
                    slots[(1, 2, 5, 6)[h]].append(("stack", r, ahead, h))
        if g == 0 and not first:
            slots[1].append(("logit", G - 2))
            slots[2].append(("xn", G - 1))
            slots[3].append(("sq", G - 1))
            slots[4].append(("rms", G - 1))
            slots[5].append(("xT", G - 1))
            slots[7].append(("logit", G - 1))
        if g == 0 and not last:
            slots[22].append(("load", 1, 0))
            slots[23].append(("load", 1, 1))
        if g == 1 and not last:
            for k, (load, scale, split) in enumerate(((None, 0, 1), (None, 0, 2), (3, 7, 8), (4, 9, 10))):
                if load:
                    slots[load].insert(0, ("load", 1, k))
                slots[scale].insert(0, ("c_scale", 1, k))
                slots[split].append(("c", 1, k))
            for k, (load, at, norm) in enumerate(((10, 15, 18), (13, 20, 23), (21, 24, 27), (26, 29, None))):
                slots[load].append(("load", 1, KC + k))
                slots[at].append(("stats", 1, k, 0))
                slots[at + 1].append(("stats", 1, k, 1))
                if norm:
                    slots[norm].append(("x_norm", 1, k))
                    slots[norm + 1].append(("norm", 1, k))
        if g == 2 and not last:
            slots[0].append(("x_norm", 1, KC - 1))
            slots[1].append(("norm", 1, KC - 1))
        e_slots = (((2, 0), (7, 3), (12, 8), (16, 13), (21, 17), (25, 22), (31, 28)),
                   ((5, 2), (22, 16), (31, 28)),
                   ((4, 0), (8, 5), (12, 9), (16, 13), (20, 17), (25, 21), (31, 28)))
        e_first = (0, 7, 10, 17)[g]
        for i, (split, load) in enumerate(e_slots[1 if g == 1 else 2 if last and g > 1 else 0]):
            slots[load].insert(0, ("e_load", e_first + i))
            slots[split].append(("e_split", e_first + i))
        return slots

    def steps(first, last):
        if not first:
            yield from merging(True)
        for g in range(G):
            slots = group_slots(g, first, last)
            for u in range(UNITS):
                yield from slots[u]
                yield ("st", g, u)
                s = UNITS * (g + 1) + u + LEAD
                rs, gs, us = s // (UNITS * G), s // UNITS % G, s % UNITS
                if not (last and rs == 1):
                    yield ("s", rs, gs, us)
                    if us == UNITS - 1:
                        yield ("combine", rs, gs)
                if u > 1:
                    yield ("pv", g, u // 2 - 1, u % 2)
                if u == UNITS - LEAD + 2:
                    rs, gs = (g + 1) // G, (g + 1) % G
                    if not (last and rs == 1):
                        yield ("mxT", rs, gs)
                        yield ("shift", rs, gs)
                if u == UNITS // 2 + 1:
                    yield ("take", g, 0)
            yield ("pv", g, UNITS // 2 - 1, 0)
            yield ("pv", g, UNITS // 2 - 1, 1)
            yield ("take", g, 1)

    def merging(values):
        if values:
            for t in range(2):
                yield ("v", t)
        yield ("den", -1, G - 1)
        yield ("resid", 0)
        if values:
            for t in range(2, 4):
                yield ("v", t)
        yield ("scale", -1, G - 1, 0)
        yield ("scale", -1, G - 1, 1)
        yield ("resid", 1)
        yield ("out", -1, G - 1)
        if values:
            for t in range(4, 6):
                yield ("v", t)
        for o in range(G + 1):
            if o < G:
                yield ("merge", o)
                yield ("x1", o)
                if o + 2 < G:
                    yield ("resid", o + 2)
                yield ("x1_stats", o)
            if o >= 2 and not (values and o == G):
                yield ("logit", o - 2)
            if values and o < G:
                yield ("stack", 0, 1, o)
            if o >= 1:
                if not (values and o == G):
                    yield ("xn", o - 1)
                if values and o in (1, 2):
                    yield ("v", 5 + o)
                if not (values and o == G):
                    yield ("xT", o - 1)
                    yield ("sq", o - 1)
                    yield ("rms", o - 1)
        if not values:
            yield ("logit", G - 1)

    def opening():
        for k in range(KC):
            yield ("load", 0, k)
            yield ("c_scale", 0, k)
            yield ("c", 0, k)
        for k in range(KC):
            yield ("load", 0, KC + k)
            yield ("stats", 0, k, 0)
            yield ("stats", 0, k, 1)
            yield ("x_norm", 0, k)
            yield ("norm", 0, k)
        for _, step in sorted(rope_steps(0, 0, 0), key=lambda item: item[0]):
            yield step
            if step[0] == "qk":
                for t in range(NT):
                    yield ("v", t)
        for h in range(HG):
            yield ("stack", 0, 0, h)
        slots = [[] for _ in range(UNITS)]
        for at, step in rope_steps(0, 1, 0):
            slots[at].append(step)
        for u in range(UNITS):
            yield from slots[u]
            yield ("s", 0, 0, u)
        for h in range(HG):
            yield ("stack", 0, 1, h)
        yield ("combine", 0, 0)
        yield ("mxT", 0, 0)
        yield ("shift", 0, 0)
        for u in range(LEAD):
            yield ("s", 0, 1, u)

    def work_items(step):
        n = {"v": 1, "merge": 2, "xT": 2, "logit": 1, "qk": 4, "s": 2, "mxT": 1}.get(step[0], 0)
        return [(*step, i) for i in range(n)]

    bodies = {"opening": list(opening()), "closing": list(merging(False)),
              "first": list(steps(True, False)), "middle": list(steps(False, False)),
              "last": list(steps(False, True))}
    order = {name: [item for step in body for item in work_items(step)] for name, body in bodies.items()}
    place, at = {}, 0
    for name in ("opening", "first", "middle", "last", "closing"):
        place[name] = {item: (at + i) % 2 for i, item in enumerate(order[name])}
        at += len(order[name])
    assert len(order["middle"]) % 2 == 0

    def walk(eng, program):
        program("opening", 0)
        program("first", 0)
        if B > 2:
            with eng.Fori(1, B - 1) as b:
                program("middle", b)
        program("last", B - 1)
        program("closing", B)

    with ExitStack() as ctx:
        def sb(name, shape, dt=F32):
            return ctx.enter_context(nc.sbuf_tensor(name, shape, dt))

        def ps(name, shape, dt=F32):
            return ctx.enter_context(nc.psum_tensor(name, shape, dt))

        def sem(name):
            return ctx.enter_context(nc.semaphore(name))

        w_hi = {w: sb(f"{w}_hi", [P, KC, C], F16) for w in ("wq", "wk", "wv", "wm")}
        w_lo = {w: sb(f"{w}_lo", [P, KC, C], F16) for w in ("wq", "wk", "wv", "wm")}
        rope_cos = sb("rope_cos", [P, N])
        rope_sin = sb("rope_sin", [P, N])
        stage = sb("stage", [P, 2, N])
        x_hi = sb("x_hi", [P, KC, N], F16)
        x_lo = sb("x_lo", [P, KC, N], F16)
        c_hi = sb("c_hi", [P, KC, N], F16)
        c_lo = sb("c_lo", [P, KC, N], F16)
        o_hi = sb("o_hi", [P, G, N], F16)
        o_lo = sb("o_lo", [P, G, N], F16)
        qk_f = sb("qk_f", [P, 2, N])
        qk_sw = sb("qk_sw", [P, N])
        qk_hi = sb("qk_hi", [P, 2, 2, N], F16)
        qk_lo = sb("qk_lo", [P, 2, N], F16)
        q_stack = sb("q_stack", [P, 2, HG, N], F16)
        k_stack = sb("k_stack", [P, 2, HG, N], F16)
        v_t = sb("v_t", [P, NT, C])
        probs = sb("probs", [P, 4, N])
        pv_raw = sb("pv_raw", [P, N])
        pv_den = sb("pv_den", [P, 2, N])
        den = sb("den", [P, N // HD])
        mx_half = sb("mx_half", [P, 2, UNITS])
        mx = sb("mx", [P, UNITS])
        neg_mx = sb("neg_mx", [UNITS, P], F16)
        ones = sb("ones", [P, HD])
        neg_half = sb("neg_half", [P, 1])
        bias_qk = sb("bias_qk", [P, 2, G])
        bias_v = sb("bias_v", [P, C])
        bias_m = sb("bias_m", [P, G])
        gate = sb("gate", [P, 2])
        gate_scale = sb("gate_scale", [P, 1])
        sign = sb("sign", [P, 1])
        stats = sb("stats", [P, 4, 2, 6])
        mean_var = sb("mean_var", [P, 4, 2])
        ln_scale = sb("ln_scale", [P, 4, 2])
        stats2 = sb("stats2", [P, 4, 2, 6])
        mean_var2 = sb("mean_var2", [P, 4, 2])
        ln_scale2 = sb("ln_scale2", [P, 4, 2])
        sq_sum = sb("sq_sum", [P, 4])
        e_raw = sb("e_raw", [P, EW])
        e_part = sb("e_part", [P, 2, EW], F16)
        router_raw = sb("router_raw", [P, FC, E])
        router_scale = sb("router_scale", [P, FC])
        router_w = sb("router_w", [P, FC, E])
        rms = sb("rms", [P, 4, 1])
        ident = keep["ident"]
        logits = keep["logits"]

        work = [ps(f"work{i}", [P, HALF]) for i in range(2)]
        st_ps = [ps(f"st_ps{i}", [P, N]) for i in range(2)]
        pv_ps = ps("pv_ps", [P, N])

        stage_full = [sem(f"stage_full{i}") for i in range(2)]
        resid_full = [sem(f"resid_full{i}") for i in range(2)]
        const_full = sem("const_full")
        wload_full = [sem(f"wload_full{i}") for i in range(4)]
        setup_pool = sem("setup_pool")
        setup_act = sem("setup_act")
        setup_dve = sem("setup_dve")
        w_hi_done = sem("w_hi_done")
        w_lo_done = sem("w_lo_done")
        ln_chain = sem("ln_chain")
        ln_ready = sem("ln_ready")
        ln_half = sem("ln_half")
        ln_stats = sem("ln_stats")
        ln2_half = sem("ln2_half")
        ln2_stats = sem("ln2_stats")
        rms_ready = sem("rms_ready")
        x_norm = sem("x_norm")
        x_hi_done = sem("x_hi_done")
        x_lo_done = sem("x_lo_done")
        c_scaled = sem("c_scaled")
        c_hi_done = sem("c_hi_done")
        c_lo_done = sem("c_lo_done")
        v_ps_full = sem("v_ps_full")
        v_done = sem("v_done")
        qk_ps_full = sem("qk_ps_full")
        qk_evac = sem("qk_evac")
        swapped = sem("swapped")
        cos_done = sem("cos_done")
        sin_done = sem("sin_done")
        rope_sum = sem("rope_sum")
        qk_hi_done = sem("qk_hi_done")
        qk_lo_done = sem("qk_lo_done")
        stacked = [sem(f"stacked{i}") for i in range(2)]
        s_full = sem("s_full")
        s_maxed = sem("s_maxed")
        mx_done = sem("mx_done")
        mxT_full = sem("mxT_full")
        neg_done = sem("neg_done")
        shift_in = sem("shift_in")
        st_full = sem("st_full")
        exp_done = sem("exp_done")
        pv_step = sem("pv_step")
        pv_evac = sem("pv_evac")
        taken = sem("taken")
        den_out = sem("den_out")
        den_in = sem("den_in")
        recip_done = sem("recip_done")
        recip_out = sem("recip_out")
        recip_in = sem("recip_in")
        out_scaled = sem("out_scaled")
        out_norm = sem("out_norm")
        out_hi = sem("out_hi")
        out_lo = sem("out_lo")
        merge_full = sem("merge_full")
        biased = sem("biased")
        x1_done = sem("x1_done")
        x1_stored = [sem(f"x1_stored{i}") for i in range(2)]
        ln2_chain = sem("ln2_chain")
        ln2_ready = sem("ln2_ready")
        xn_done = sem("xn_done")
        sq_done = sem("sq_done")
        xn_stored = sem("xn_stored")
        xT_full = sem("xT_full")
        xT_evac = sem("xT_evac")
        logit_full = sem("logit_full")
        logit_done = sem("logit_done")
        e_in = sem("e_in")
        e_scaled = sem("e_scaled")
        e_hi_done = sem("e_hi_done")
        e_lo_done = sem("e_lo_done")
        e_out = sem("e_out")
        rms_chain = sem("rms_chain")

        def emptied_by(b, item):
            kind, i = item[0], item[-1]
            if kind == "v":
                return v_done, b * NT + item[1] + 1
            if kind == "qk":
                return qk_evac, (b + item[1]) * (4 * G) + 4 * item[2] + i + 1
            if kind == "s":
                return s_maxed, (b + item[1]) * (2 * UNITS * G) + 2 * UNITS * item[2] + 2 * item[3] + i + 1
            if kind == "mxT":
                return neg_done, (b + item[1]) * G + item[2] + 1
            if kind == "merge":
                return x1_done, (b - 1) * (2 * G) + 2 * item[1] + i + 1
            if kind == "xT":
                return xT_evac, (b - 1) * (2 * G) + 2 * item[1] + i + 1
            return logit_done, (b - 1) * G + item[1] + 1

        def resid_at(o):
            return pv_raw[:] if o % 2 == 0 else pv_den[:, 1, :]

        def ropes_before(b):
            done = b * (2 * G) + 2 * G
            return done if isinstance(b, int) and b == B - 1 else done + 4

        NCONST = 9
        W_ORDER = ("wv", "wk", "wq", "wm")

        def landing(i):
            return (stage[:] if i % 2 == 0 else probs[:, 0:2, :]).rearrange("p a n -> p (a n)")[:, 0:KC * C]

        block = ctx.enter_context(nc.Block())

        @block.sync
        def _(sp):
            alone = keep["alone"]
            for dst, src in ((rope_cos[:], dram["cos"]), (rope_sin[:], dram["sin"]),
                             (bias_qk[:], dram["bias_qk"]), (bias_v[:], dram["bias_v"]),
                             (bias_m[:], dram["bias_m"]), (gate[:], dram["gates"]), (sign[:], dram["sign"]),
                             (router_raw[:], dram["router"]), (router_scale[:], dram["router_scale"])):
                sp.dma_start(dst, src).then_inc(const_full, 16)
            for i, w in enumerate(W_ORDER):
                if i >= 2:
                    sp.wait_ge(w_lo_done, i - 1)
                sp.dma_start(landing(i).rearrange("p (k c) -> p k c", k=KC),
                             dram[w].rearrange("(k p) c -> p k c", p=P)).then_inc(wload_full[i], 16)
            sp.wait_ge(w_lo_done, 4)

            def chunk(name, b, k):
                if isinstance(b, int):
                    return dram[name][b, k * P:(k + 1) * P, :]
                return dram[name][bass.ds(b, 1), k * P:(k + 1) * P, :].rearrange("b p n -> p (b n)")

            def load(b, n):
                if n < 2:
                    sp.wait_ge(x_lo_done, b * KC)
                    alone(sp)
                    if n == 0 and not (isinstance(b, int) and b == 0):
                        sp.wait_ge(logit_full, (b - 1) * G)
                        alone(sp)
                elif n < KC + 2:
                    sp.wait_ge(c_lo_done, b * KC + n - 1)
                else:
                    sp.wait_ge(x_lo_done, b * KC + n - KC - 1)
                alone(sp)
                sp.dma_start(stage[:, n % 2, :], chunk("ctx" if n < KC else "x", b, n % KC)
                             ).then_inc(stage_full[n % 2], 16)

            def stack(b, g, h):
                par = g % 2
                if h == 0:
                    sp.wait_ge(qk_lo_done, b * (2 * G) + 2 * g + 2)
                    alone(sp)
                    if g >= 2:
                        sp.wait_ge(st_full, b * (UNITS * G) + UNITS * (g - 1))
                    elif not (isinstance(b, int) and b == 0):
                        sp.wait_ge(st_full, b * (UNITS * G) - UNITS * (1 - g))
                    alone(sp)
                rows = slice(HD * h, HD * h + HD)
                for row, part in enumerate((qk_hi[:, par], qk_lo, qk_hi[:, par])):
                    sp.dma_start(k_stack[HD * row:HD * row + HD, par, h, :], part[rows, 0, :]
                                 ).then_inc(stacked[par], 16)
                for row, part in enumerate((qk_hi[:, par], qk_hi[:, par], qk_lo)):
                    sp.dma_start(q_stack[HD * row:HD * row + HD, par, h, :], part[rows, 1, :]
                                 ).then_inc(stacked[par], 16)

            def shift(b, g):
                sp.wait_ge(neg_done, b * G + g + 1)
                alone(sp)
                sp.dma_start(dram["shift"][g % 2], neg_mx[:]).then_inc(shift_in, 16)
                sp.wait_ge(shift_in, (b * G + g) * 32 + 16)
                alone(sp)
                sp.dma_start(q_stack[3 * HD:3 * HD + 1, g % 2, :, :].rearrange("o h n -> o (h n)"),
                             dram["shift"][g % 2].rearrange("(o u) p -> o (u p)", o=1)).then_inc(shift_in, 16)

            def take(b, g, pair):
                if pair == 0:
                    if g >= 1:
                        sp.wait_ge(out_norm, b * G + g)
                    else:
                        sp.wait_ge(x1_done, b * (2 * G))
                    alone(sp)
                sp.wait_ge(pv_evac, b * (2 * G) + 2 * g + pair + 1)
                alone(sp)
                for j in range(2):
                    h = 2 * pair + j
                    sp.dma_start(dram["den"][h:h + 1, :], pv_raw[64 * j + HD:64 * j + HD + 1, :]).then_inc(den_out, 16)
                for j in range(2):
                    to = slice(HD * (2 * pair + j), HD * (2 * pair + j) + HD)
                    sp.dma_start(pv_den[to, 0, :], pv_raw[64 * j:64 * j + HD, :]).then_inc(taken, 16)
                if pair == 1:
                    sp.wait_ge(den_out, (b * G + g + 1) * 64)
                    alone(sp)
                    sp.dma_start(den[:], dram["den"].rearrange("h (p c) -> (h p) c", c=N // HD)).then_inc(den_in, 16)

            def den_back(b, g):
                n = b * G + g
                sp.wait_ge(recip_done, n + 1)
                alone(sp)
                sp.dma_start(dram["recip"], den[:]).then_inc(recip_out, 16)
                sp.wait_ge(recip_out, (n + 1) * 16)
                alone(sp)
                for h in range(HG):
                    row = dram["recip"][HD * h:HD * h + HD, :].rearrange("(o p) c -> o (p c)", o=1)
                    sp.dma_start(pv_den[HD * h:HD * h + HD, 1, :], row.to_broadcast([HD, N])).then_inc(recip_in, 16)

            def load_expert(n):
                sp.wait_ge(e_lo_done, n)
                alone(sp)
                sp.dma_start(e_raw[:], dram["w_raw_pieces"][:, bass.ds(n, 1), :].rearrange("p c n -> p (c n)")
                             ).then_inc(e_in, 16)

            def store_expert(n):
                sp.wait_ge(e_lo_done, n + 1)
                alone(sp)
                sp.dma_start(dram["w_split_pieces"][:, bass.ds(n, 1), :].rearrange("p c n -> p (c n)"),
                             e_part[:].rearrange("p l n -> p (l n)")).then_inc(e_out, 16)

            def resid(b, o):
                if o == 0:
                    sp.wait_ge(taken, (b + 1) * (64 * G))
                    alone(sp)
                    sp.wait_ge(den_out, (b + 1) * (64 * G))
                elif o == 1:
                    sp.wait_ge(out_scaled, (b + 1) * (2 * G))
                else:
                    sp.wait_ge(x1_done, b * (2 * G) + 2 * (o - 1))
                alone(sp)
                sp.dma_start(resid_at(o), chunk("x", b, o)).then_inc(resid_full[o % 2], 16)

            def store_x1(b, o):
                sp.wait_ge(x1_done, b * (2 * G) + 2 * o + 2)
                alone(sp)
                sp.dma_start(chunk("x1", b, o), qk_f[:, o % 2, :]).then_inc(x1_stored[o % 2], 16)

            def store_xn(b, o):
                sp.wait_ge(xn_done, b * G + o + 1)
                alone(sp)
                sp.dma_start(chunk("xn", b, o), qk_sw[:]).then_inc(xn_stored, 16)

            def program(name, b):
                for step in bodies[name]:
                    kind = step[0]
                    if kind == "load":
                        load(b + step[1], step[2])
                    elif kind == "stack":
                        stack(b + step[1], *step[2:])
                    elif kind == "shift":
                        shift(b + step[1], step[2])
                    elif kind == "resid":
                        resid(b - 1, step[1])
                    elif kind == "x1":
                        store_x1(b - 1, step[1])
                    elif kind == "xn":
                        store_xn(b - 1, step[1])
                    elif kind == "take":
                        take(b, *step[1:])
                    elif kind == "den":
                        den_back(b + step[1], step[2])
                    elif kind == "e_load":
                        n = b * CB + step[1]
                        if step[1] > 0:
                            store_expert(n - 1)
                        load_expert(n)
                if name not in ("opening", "closing"):
                    store_expert(b * CB + CB - 1)

            walk(sp, program)
            sp.wait_ge(xn_stored, 16 * B * G)
            sp.wait_ge(e_out, 16 * B * CB)
            for r in range(2):
                sp.wait_ge(x1_stored[r], 16 * B * (G // 2))

        @block.gpsimd
        def _(pool):
            alone = keep["alone"]
            pool.wait_ge(setup_dve, 2)
            pool.memset(ones[:], 1.0).then_inc(setup_pool, 1)
            pool.wait_ge(setup_pool, 1)
            pool.memset(k_stack[3 * HD:4 * HD, :, :, :], S_ACT * S_ACT).then_inc(setup_pool, 1)
            pool.wait_ge(setup_pool, 2)
            pool.memset(neg_half[:], -0.5).then_inc(setup_pool, 1)
            pool.wait_ge(setup_pool, 3)

            def scale_and_shift(mv, out, i, have, chain, done, n, scale):
                pool.wait_ge(have, n + 1)
                alone(pool)
                pool.tensor_scalar(out[:, i, 0:1], mv[:, i, 1:2], LN_EPS, scale ** -2, ALU.add, ALU.mult
                                   ).then_inc(chain, 1)
                pool.wait_ge(chain, n * 2 + 1)
                pool.tensor_tensor(out[:, i, 0:1], out[:, i, 0:1], neg_half[:], ALU.pow).then_inc(chain, 1)
                pool.wait_ge(chain, n * 2 + 2)
                alone(pool)
                pool.tensor_scalar(out[:, i, 1:2], mv[:, i, 0:1], out[:, i, 0:1], -1.0, ALU.mult, ALU.mult
                                   ).then_inc(done, 1)

            def c_low(b, k):
                pool.wait_ge(c_hi_done, b * KC + k + 1)
                pool.tensor_tensor(c_lo[:, k, :], stage[:, k % 2, :], c_hi[:, k, :], ALU.subtract).then_inc(c_lo_done, 1)

            def x_low(b, k):
                pool.wait_ge(x_hi_done, b * KC + k + 1)
                pool.tensor_tensor(x_lo[:, k, :], stage[:, k % 2, :], x_hi[:, k, :], ALU.subtract).then_inc(x_lo_done, 1)

            def rotate(b, g, i):
                n = b * (2 * G) + 2 * g + i + 1
                pool.wait_ge(swapped, 2 * n)
                pool.tensor_tensor(qk_f[:, i, :], qk_f[:, i, :], rope_cos[:], ALU.mult).then_inc(cos_done, 1)
                pool.tensor_tensor(qk_sw[:], qk_sw[:], rope_sin[:], ALU.mult).then_inc(sin_done, 1)

            def qk_low(b, g, i):
                n = b * (2 * G) + 2 * g + i + 1
                pool.wait_ge(qk_hi_done, n)
                if i == 0 and (g >= 1 or not (isinstance(b, int) and b == 0)):
                    pool.wait_ge(stacked[(g - 1) % 2], (b * (G // 2) + (g + 1) // 2) * (24 * 16))
                pool.tensor_tensor(qk_lo[:, i, :], qk_f[:, i, :], qk_hi[:, g % 2, i, :], ALU.subtract
                                   ).then_inc(qk_lo_done, 1)

            def out_low(b, g):
                pool.wait_ge(out_hi, b * G + g + 1)
                pool.tensor_tensor(o_lo[:, g, :], pv_den[:, 0, :], o_hi[:, g, :], ALU.subtract).then_inc(out_norm, 1)

            def token_rms(b, o):
                n = b * G + o
                pool.wait_ge(sq_done, n + 1)
                alone(pool)
                pool.tensor_scalar(rms[:, o, :], sq_sum[:, o:o + 1], N * 1e-6, None, ALU.add).then_inc(rms_chain, 1)
                pool.wait_ge(rms_chain, n + 1)
                pool.tensor_tensor(rms[:, o, :], rms[:, o, :], neg_half[:], ALU.pow).then_inc(rms_ready, 1)

            def program(name, b):
                for step in bodies[name]:
                    kind = step[0]
                    if kind == "c":
                        c_low(b + step[1], step[2])
                    elif kind == "stats" and step[3] == 1:
                        scale_and_shift(mean_var, ln_scale, step[2], ln_stats, ln_chain, ln_ready,
                                        (b + step[1]) * KC + step[2], S_ACT)
                    elif kind == "norm":
                        x_low(b + step[1], step[2])
                    elif kind == "swap" and step[4] == 1:
                        rotate(b + step[1], step[2], step[3])
                    elif kind == "hi":
                        qk_low(b + step[1], *step[2:])
                    elif kind == "out":
                        if step[1] == 0:
                            out_low(b, step[2])
                    elif kind == "x1_stats":
                        scale_and_shift(mean_var2, ln_scale2, step[1], ln2_stats, ln2_chain, ln2_ready,
                                        (b - 1) * G + step[1], 1.0)
                    elif kind == "rms":
                        token_rms(b - 1, step[1])
                    elif kind == "e_split":
                        n = b * CB + step[1]
                        pool.wait_ge(e_hi_done, n + 1)
                        pool.tensor_tensor(e_part[:, 1, :], e_raw[:], e_part[:, 0, :], ALU.subtract
                                           ).then_inc(e_lo_done, 1)

            walk(pool, program)

        @block.scalar
        def _(act):
            act.wait_ge(const_full, 16 * NCONST)
            act.activation(gate[:], gate[:], ACT.Tanh).then_inc(setup_act, 1)
            act.wait_ge(setup_act, 1)
            act.mul(gate_scale[:], gate[:, 0:1], inv_ps).then_inc(setup_act, 1)
            act.mul(bias_m[:], bias_m[:], gate[:, 0:1]).then_inc(setup_act, 1)
            act.wait_ge(setup_act, 3)
            for i, w in enumerate(W_ORDER):
                act.wait_ge(wload_full[i], 16)
                act.activation(w_hi[w][:].rearrange("p k c -> p (k c)"), landing(i), ACT.Copy, scale=S_W
                               ).then_inc(w_hi_done, 1)

            def c_scale(b, k):
                act.wait_ge(stage_full[k % 2], (b * 4 + k // 2 + 1) * 16)
                act.activation(stage[:, k % 2, :], stage[:, k % 2, :], ACT.Copy, scale=S_ACT).then_inc(c_scaled, 1)

            def c_high(b, k):
                act.wait_ge(c_scaled, b * KC + k + 1)
                if k == 0 and not (isinstance(b, int) and b == 0):
                    act.wait_ge(qk_ps_full, b * (4 * G))
                act.activation(c_hi[:, k, :], stage[:, k % 2, :], ACT.Copy).then_inc(c_hi_done, 1)

            def x_normalise(b, k):
                act.wait_ge(ln_ready, b * KC + k + 1)
                act.activation(stage[:, k % 2, :], stage[:, k % 2, :], ACT.Identity, scale=ln_scale[:, k, 0:1],
                               bias=ln_scale[:, k, 1:2]).then_inc(x_norm, 1)

            def x_high(b, k):
                act.wait_ge(x_norm, b * KC + k + 1)
                act.activation(x_hi[:, k, :], stage[:, k % 2, :], ACT.Copy).then_inc(x_hi_done, 1)

            def evac_qk(bank, b, g):
                for i in range(2):
                    for half in range(2):
                        act.wait_ge(qk_ps_full, b * (4 * G) + 4 * g + 2 * i + half + 1)
                        if half == 0 and not (isinstance(b, int) and b == 0 and g == 0):
                            act.wait_ge(qk_lo_done, b * (2 * G) + 2 * g + i - 1)
                        if half == 0 and g == 2:
                            act.wait_ge(x1_stored[i], b * (G // 2) * 16)
                        act.activation(qk_f[:, i, half * HALF:(half + 1) * HALF], bank(2 * i + half)[:],
                                       ACT.Identity, scale=inv_ps, bias=bias_qk[:, 1 - i, g:g + 1]
                                       ).then_inc(qk_evac, 1)

            def exps(b, g, u):
                n = UNITS * g + u
                act.wait_ge(st_full, b * (UNITS * G) + n + 1)
                if n >= 4 or not (isinstance(b, int) and b == 0):
                    act.wait_ge(pv_step, b * (UNITS // 2 * G) + n // 2 - 1)
                act.activation(probs[:, u % 4, :], st_ps[u % 2][:], ACT.Exp, scale=1.0 / (S_ACT * S_ACT * HD ** 0.5)
                               ).then_inc(exp_done, 1)

            def evac_pv(b, g, pair):
                n = b * (2 * G) + 2 * g + pair
                act.wait_ge(pv_step, b * (UNITS // 2 * G) + (UNITS // 2) * g + (UNITS // 4) * (pair + 1))
                act.wait_ge(taken, n * 32)
                act.wait_ge(den_out, n * 32)
                if g == 0 and pair == 0:
                    act.wait_ge(x1_done, b * (2 * G))
                act.activation(pv_raw[:], pv_ps[:], ACT.Copy).then_inc(pv_evac, 1)

            def add_bias(b, o):
                act.wait_ge(resid_full[o % 2], (b * (G // 2) + o // 2) * 16 + 16)
                act.activation(resid_at(o), resid_at(o), ACT.Identity, bias=bias_m[:, o:o + 1]).then_inc(biased, 1)

            def normed(b, o):
                act.wait_ge(ln2_ready, b * G + o + 1)
                act.wait_ge(xn_stored, (b * G + o) * 16)
                if o >= 1:
                    act.wait_ge(xT_full, b * (2 * G) + 2 * o)
                    act.wait_ge(sq_done, b * G + o)
                act.activation(qk_sw[:], qk_f[:, o % 2, :], ACT.Identity, scale=ln_scale2[:, o, 0:1],
                               bias=ln_scale2[:, o, 1:2]).then_inc(xn_done, 1)

            def squared(b, o, ready):
                act.wait_ge(xn_done, b * G + o + 1)
                act.wait_ge(x_lo_done, ready * KC)
                act.activation(stage[:, 0, :], qk_sw[:], ACT.Square, accum_out=sq_sum[:, o:o + 1]
                               ).then_inc(sq_done, 1)

            def program(name, b):
                for step in bodies[name]:
                    kind = step[0]

                    def bank(i):
                        return work[place[name][(*step, i)]]

                    if kind == "c_scale":
                        c_scale(b + step[1], step[2])
                    elif kind == "c":
                        c_high(b + step[1], step[2])
                    elif kind == "x_norm":
                        x_normalise(b + step[1], step[2])
                    elif kind == "norm":
                        x_high(b + step[1], step[2])
                    elif kind == "qk":
                        evac_qk(bank, b + step[1], step[2])
                    elif kind == "st":
                        exps(b, *step[1:])
                    elif kind == "take":
                        evac_pv(b, *step[1:])
                    elif kind == "merge":
                        add_bias(b - 1, step[1])
                    elif kind == "xn":
                        normed(b - 1, step[1])
                    elif kind == "sq":
                        squared(b - 1, step[1], B if name == "closing" else b + 1)
                    elif kind == "e_split":
                        n = b * CB + step[1]
                        act.wait_ge(e_in, (n + 1) * 16)
                        act.wait_ge(e_out, n * 16)
                        act.activation(e_raw[:], e_raw[:], ACT.Copy, scale=S_E).then_inc(e_scaled, 1)
                        act.wait_ge(e_scaled, n + 1)
                        act.activation(e_part[:, 0, :], e_raw[:], ACT.Copy).then_inc(e_hi_done, 1)

            walk(act, program)

        @block.vector
        def _(dve):
            alone = keep["alone"]
            dve.wait_ge(const_full, 16 * NCONST)
            dve.tensor_scalar(rope_cos[:], rope_cos[:], S_ACT, None, ALU.mult).then_inc(setup_dve, 1)
            dve.tensor_scalar(rope_sin[:], rope_sin[:], sign[:, 0:1], S_ACT, ALU.mult, ALU.mult).then_inc(setup_dve, 1)
            for k in range(FC):
                dve.tensor_scalar(router_w[:, k, :], router_raw[:, k, :], router_scale[:, k:k + 1], None,
                                  ALU.mult).then_inc(setup_dve, 1)
            for i, w in enumerate(W_ORDER):
                dve.wait_ge(w_hi_done, i + 1)
                dve.scalar_tensor_tensor(out=w_lo[w][:].rearrange("p k c -> p (k c)"), in0=landing(i), scalar=S_W,
                                         in1=w_hi[w][:].rearrange("p k c -> p (k c)"), op0=ALU.mult,
                                         op1=ALU.subtract).then_inc(w_lo_done, 1)

            def stats_half(src, st, i, half, half_done):
                dve.bn_stats(st[:, i, half, :], src[:, half * HALF:(half + 1) * HALF]).then_inc(half_done, 1)

            def aggregate(st, mv, i, half_done, done, n):
                dve.wait_ge(half_done, n * 2 + 2)
                alone(dve)
                dve.bn_aggr(mv[:, i, :], st[:, i, :, :].rearrange("p a s -> p (a s)")).then_inc(done, 1)

            def stats_x(b, k, half):
                dve.wait_ge(stage_full[k % 2], (b * 4 + 2 + k // 2 + 1) * 16)
                stats_half(stage[:, k % 2, :], stats, k, half, ln_half)
                if half == 1:
                    aggregate(stats, mean_var, k, ln_half, ln_stats, b * KC + k)

            def merged(bank, b, o):
                dve.wait_ge(biased, b * G + o + 1)
                if o < 2:
                    dve.wait_ge(qk_lo_done, ropes_before(b))
                else:
                    dve.wait_ge(x1_stored[o % 2], (b * (G // 2) + o // 2) * 16)
                    dve.wait_ge(xn_done, b * G + o - 1)
                for half in range(2):
                    dve.wait_ge(merge_full, b * (2 * G) + 2 * o + half + 1)
                    dve.scalar_tensor_tensor(out=qk_f[:, o % 2, cols_of(half)], in0=bank(half)[:],
                                             scalar=gate_scale[:, 0:1], in1=resid_at(o)[:, cols_of(half)],
                                             op0=ALU.mult, op1=ALU.add).then_inc(x1_done, 1)

            def stats_x1(b, o):
                dve.wait_ge(x1_done, b * (2 * G) + 2 * o + 2)
                for half in range(2):
                    stats_half(qk_f[:, o % 2, :], stats2, o, half, ln2_half)
                aggregate(stats2, mean_var2, o, ln2_half, ln2_stats, b * G + o)

            def value(bank, b, t):
                dve.wait_ge(v_ps_full, b * NT + t + 1)
                dve.scalar_tensor_tensor(out=v_t[:, t, :], in0=bank(0)[:], scalar=inv_ps,
                                         in1=bias_v[:], op0=ALU.mult, op1=ALU.add).then_inc(v_done, 1)

            def cols_of(half):
                return slice(half * HALF, (half + 1) * HALF)

            def swap(b, g, i, half):
                dve.wait_ge(qk_evac, b * (4 * G) + 4 * g + 2 * i + half + 1)
                dve.wait_ge(rope_sum, 2 * (b * (2 * G) + 2 * g + i))
                if g == 2 and i == 0 and half == 0:
                    dve.wait_ge(xn_stored, b * G * 16)
                    dve.wait_ge(xT_full, b * (2 * G))
                    dve.wait_ge(sq_done, b * G)
                alone(dve)
                dve.stream_shuffle(qk_sw[:, cols_of(half)], qk_f[:, i, cols_of(half)], [j ^ 1 for j in range(32)]
                                   ).then_inc(swapped, 1)

            def rope_add(b, g, i, half):
                n = b * (2 * G) + 2 * g + i
                dve.wait_ge(cos_done, n + 1)
                dve.wait_ge(sin_done, n + 1)
                dve.tensor_tensor(qk_f[:, i, cols_of(half)], qk_f[:, i, cols_of(half)], qk_sw[:, cols_of(half)],
                                  ALU.add).then_inc(rope_sum, 1)

            def qk_high(b, g, i):
                dve.wait_ge(rope_sum, 2 * (b * (2 * G) + 2 * g + i) + 2)
                if i == 0 and (g >= 2 or not (isinstance(b, int) and b == 0)):
                    dve.wait_ge(stacked[g % 2], (b * (G // 2) + g // 2) * (24 * 16))
                    dve.wait_ge(s_full, b * (2 * UNITS * G) + 2 * UNITS * (g - 1))
                dve.tensor_copy(qk_hi[:, g % 2, i, :], qk_f[:, i, :]).then_inc(qk_hi_done, 1)

            def maxes(bank, b, g, u):
                nt, h = u // HG, u % HG
                for half in range(2):
                    dve.wait_ge(s_full, b * (2 * UNITS * G) + 2 * UNITS * g + 2 * u + half + 1)
                    dve.reduce_max(mx_half[:, half, h * NT + nt:h * NT + nt + 1], bank(half)[:],
                                   axis=AX.X).then_inc(s_maxed, 1)

            def combine(b, g):
                dve.wait_ge(s_maxed, b * (2 * UNITS * G) + 2 * UNITS * (g + 1))
                dve.tensor_tensor(mx[:], mx_half[:, 0, :], mx_half[:, 1, :], ALU.max).then_inc(mx_done, 1)
                dve.wait_ge(mx_done, b * G + g + 1)

            def negate(bank, b, g):
                dve.wait_ge(mxT_full, b * G + g + 1)
                dve.wait_ge(shift_in, (b * G + g) * 32)
                dve.tensor_scalar(neg_mx[:], bank(0)[0:UNITS, 0:P], -1.0 / (S_ACT * S_ACT), None, ALU.mult
                                  ).then_inc(neg_done, 1)

            def reciprocals(b, g):
                dve.wait_ge(den_in, (b * G + g + 1) * 16)
                dve.reciprocal(den[:], den[:]).then_inc(recip_done, 1)

            def scale_out(b, g, half):
                dve.wait_ge(recip_in, (b * G + g + 1) * (HG * 16))
                dve.wait_ge(taken, (b * G + g + 1) * 64)
                cols = cols_of(half)
                dve.scalar_tensor_tensor(out=pv_den[:, 0, cols], in0=pv_den[:, 0, cols], scalar=S_ACT,
                                         in1=pv_den[:, 1, cols], op0=ALU.mult, op1=ALU.mult).then_inc(out_scaled, 1)

            def out_high(b, g):
                dve.wait_ge(out_scaled, 2 * (b * G + g) + 2)
                if g == 0:
                    dve.wait_ge(merge_full, b * (2 * G))
                dve.tensor_copy(o_hi[:, g, :], pv_den[:, 0, :]).then_inc(out_hi, 1)

            def xT(bank, b, o):
                for half in range(2):
                    dve.wait_ge(xT_full, b * (2 * G) + 2 * o + half + 1)
                    if half == 0:
                        dve.wait_ge(logit_full, b * G + o)
                    dve.tensor_copy(stage[:, 1, half * HALF:(half + 1) * HALF], bank(half)[:]).then_inc(xT_evac, 1)

            def logit(bank, b, o):
                dve.wait_ge(rms_ready, b * G + o + 1)
                dve.wait_ge(logit_full, b * G + o + 1)
                dve.tensor_scalar(logits[:, bass.ds(b * G + o, 1), :].rearrange("p t e -> p (t e)"),
                                  bank(0)[:, 0:E], rms[:, o, :], None, ALU.mult).then_inc(logit_done, 1)

            def program(name, b):
                for step in bodies[name]:
                    kind = step[0]

                    def bank(i):
                        return work[place[name][(*step, i)]]

                    if kind == "stats":
                        stats_x(b + step[1], *step[2:])
                    elif kind == "v":
                        value(bank, b, step[1])
                    elif kind == "swap":
                        swap(b + step[1], *step[2:])
                    elif kind == "sum":
                        rope_add(b + step[1], *step[2:])
                    elif kind == "hi":
                        qk_high(b + step[1], *step[2:])
                    elif kind == "s":
                        maxes(bank, b + step[1], *step[2:])
                    elif kind == "combine":
                        combine(b + step[1], step[2])
                    elif kind == "mxT":
                        negate(bank, b + step[1], step[2])
                    elif kind == "den":
                        reciprocals(b + step[1], step[2])
                    elif kind == "scale":
                        scale_out(b + step[1], *step[2:])
                    elif kind == "out":
                        out_high(b + step[1], step[2])
                        if step[1] < 0:
                            dve.wait_ge(out_hi, b * G)
                            dve.tensor_tensor(o_lo[:, G - 1, :], pv_den[:, 0, :], o_hi[:, G - 1, :], ALU.subtract
                                              ).then_inc(out_norm, 1)
                    elif kind == "x1":
                        merged(lambda i: work[place[name][("merge", step[1], i)]], b - 1, step[1])
                    elif kind == "x1_stats":
                        stats_x1(b - 1, step[1])
                    elif kind == "xT":
                        xT(bank, b - 1, step[1])
                    elif kind == "logit":
                        logit(bank, b - 1, step[1])

            walk(dve, program)

        @block.tensor
        def _(pe):
            pe.wait_ge(w_lo_done, 4)
            pe.wait_ge(w_hi_done, 4)
            pe.wait_ge(setup_pool, 3)
            pe.wait_ge(setup_dve, 2 + FC)
            K = 3 * HD + 1

            def three(out, pairs):
                todo = [(l, r) for (lh, ll, rh, rl) in pairs for l, r in ((lh, rh), (lh, rl), (ll, rh))]
                for i, (l, r) in enumerate(todo):
                    last = pe.matmul(out, l, r, start=(i == 0), stop=(i == len(todo) - 1))
                return last

            def project_v(take, b, t):
                out = take(0)
                if t == 0:
                    pe.wait_ge(c_lo_done, (b + 1) * KC)
                m = slice(t * P, t * P + P)
                three(out[:], [(c_hi[:, k, m], c_lo[:, k, m], w_hi["wv"][:, k, :], w_lo["wv"][:, k, :])
                               for k in range(KC)]).then_inc(v_ps_full, 1)

            def project_qk(take, b, g):
                o = slice(g * P, g * P + P)
                for i, (w, hi, lo) in enumerate((("wk", c_hi, c_lo), ("wq", x_hi, x_lo))):
                    if i == 0:
                        pe.wait_ge(c_lo_done, (b + 1) * KC)
                    else:
                        pe.wait_ge(x_lo_done, (b + 1) * KC)
                    for half in range(2):
                        n = slice(half * HALF, (half + 1) * HALF)
                        out = take(2 * i + half)
                        three(out[:], [(w_hi[w][:, k, o], w_lo[w][:, k, o], hi[:, k, n], lo[:, k, n])
                                       for k in range(KC)]).then_inc(qk_ps_full, 1)

            def scores_for_max(take, b, g, u):
                nt, h = u // HG, u % HG
                rows = slice(HD * h, HD * h + HD)
                if u == 0:
                    pe.wait_ge(qk_hi_done, b * (2 * G) + 2 * g + 2)
                for half in range(2):
                    pe.matmul(take(half)[:], qk_hi[rows, g % 2, 1, nt * P:nt * P + P],
                              qk_hi[rows, g % 2, 0, half * HALF:(half + 1) * HALF], start=True, stop=True
                              ).then_inc(s_full, 1)

            def transpose_max(take, b, g):
                out = take(0)
                pe.wait_ge(mx_done, b * G + g + 1)
                pe.transpose(out[0:UNITS, 0:P], mx[:], ident[:]).then_inc(mxT_full, 1)

            def unit(u):
                return 2 * (u // (2 * NT)) + u % 2, (u % (2 * NT)) // 2

            def scores_T(b, g, u):
                h, mt = unit(u)
                n = UNITS * g + u
                if u == 0:
                    pe.wait_ge(stacked[g % 2], (b * (G // 2) + g // 2 + 1) * (24 * 16))
                    pe.wait_ge(shift_in, (b * G + g + 1) * 32)
                if n >= 2 or not (isinstance(b, int) and b == 0):
                    pe.wait_ge(exp_done, b * (UNITS * G) + n - 1)
                for half in range(2):
                    cols = slice(half * HALF, (half + 1) * HALF)
                    last = pe.matmul(st_ps[u % 2][:, cols], k_stack[0:K, g % 2, h, mt * P:mt * P + P],
                                     q_stack[0:K, g % 2, h, cols], start=True, stop=True)
                last.then_inc(st_full, 1)

            def prob_v(b, g, d, half):
                _, mt = unit(2 * d)
                pair = d // NT
                n = (UNITS // 2) * g + d
                if half == 0:
                    pe.wait_ge(exp_done, b * (UNITS * G) + 2 * n + 2)
                    if mt == 0:
                        pe.wait_ge(pv_evac, b * (2 * G) + 2 * g + pair)
                        if g == 0 and pair == 0:
                            pe.wait_ge(v_done, (b + 1) * NT)
                cols = slice(half * HALF, (half + 1) * HALF)
                for j in range(2):
                    c = g * P + (2 * pair + j) * HD
                    r = probs[:, (2 * d + j) % 4, cols]
                    pe.matmul(pv_ps[64 * j:64 * j + HD, cols], v_t[:, mt, c:c + HD], r,
                              start=(mt == 0), stop=(mt == NT - 1))
                    last = pe.matmul(pv_ps[64 * j + HD:64 * j + 2 * HD, cols], ones[:], r,
                                     start=(mt == 0), stop=(mt == NT - 1))
                if half == 1:
                    last.then_inc(pv_step, 1)

            def merge(take, b, o):
                oo = slice(o * P, o * P + P)
                if o == 0:
                    pe.wait_ge(out_norm, (b + 1) * G - 1)
                def part(out, half, ks):
                    cols = slice(half * HALF, (half + 1) * HALF)
                    for k in ks:
                        for i, (l, r) in enumerate(((w_hi["wm"], o_hi), (w_hi["wm"], o_lo), (w_lo["wm"], o_hi))):
                            last = pe.matmul(out[:], l[:, k, oo], r[:, k, cols], start=(k == 0 and i == 0),
                                             stop=(k == KC - 1 and i == 2))
                    return last

                if o == 0:
                    banks = [take(half) for half in range(2)]
                    for half in range(2):
                        part(banks[half], half, range(KC - 1))
                    pe.wait_ge(out_norm, (b + 1) * G)
                    for half in range(2):
                        part(banks[half], half, (KC - 1,)).then_inc(merge_full, 1)
                else:
                    for half in range(2):
                        part(take(half), half, range(KC)).then_inc(merge_full, 1)

            def transpose_xn(take, b, o):
                pe.wait_ge(xn_done, b * G + o + 1)
                for half in range(2):
                    out = take(half)
                    for j in range(4):
                        f = (4 * half + j) * P
                        last = pe.transpose(out[:, j * P:(j + 1) * P], qk_sw[:, f:f + P], ident[:])
                    last.then_inc(xT_full, 1)

            def router_logits(take, b, o):
                out = take(0)
                pe.wait_ge(xT_evac, b * (2 * G) + 2 * o + 2)
                for k in range(FC):
                    last = pe.matmul(out[:, 0:E], stage[:, 1, k * P:(k + 1) * P], router_w[:, k, :],
                                     start=(k == 0), stop=(k == FC - 1))
                last.then_inc(logit_full, 1)

            def program(name, b):
                seen = []
                if name == "closing":
                    seen = [emptied_by(b - 1, item) for item in order["last"][-2:]]
                elif name != "opening":
                    seen = [emptied_by(b, ("s", 0, 1, LEAD - 1, half)) for half in range(2)]
                for step in bodies[name]:
                    kind = step[0]

                    def take(i):
                        item = (*step, i)
                        if len(seen) >= 2:
                            pe.wait_ge(*seen[-2])
                        seen.append(emptied_by(b, item))
                        return work[place[name][item]]

                    if kind == "v":
                        project_v(take, b, step[1])
                    elif kind == "qk":
                        project_qk(take, b + step[1], step[2])
                    elif kind == "s":
                        scores_for_max(take, b + step[1], *step[2:])
                    elif kind == "mxT":
                        transpose_max(take, b + step[1], step[2])
                    elif kind == "st":
                        scores_T(b, *step[1:])
                    elif kind == "pv":
                        prob_v(b, *step[1:])
                    elif kind == "merge":
                        merge(take, b - 1, step[1])
                    elif kind == "xT":
                        transpose_xn(take, b - 1, step[1])
                    elif kind == "logit":
                        router_logits(take, b - 1, step[1])

            walk(pe, program)
S_X = 64.0
S_H = 64.0
TOP_K = 2


def routing_phase(nc, keep, dram, shapes):
    T, E = shapes["T"], shapes["E"]
    MAXT = shapes["MAXT"]
    with ExitStack() as ctx:
        def sb(name, shape, dt=F32):
            return ctx.enter_context(nc.sbuf_tensor(name, shape, dt))

        def sem(name):
            return ctx.enter_context(nc.semaphore(name))

        logits = keep["logits"]
        iota_m = sb("iota_m", [P, E])
        scale_e = sb("scale_e", [P, E])
        gates = sb("gates_r", [P, 2])
        gate_t = sb("gate_t", [P, 1])
        tri = sb("tri", [P, P])
        ones = sb("ones_r", [P, P])
        token = sb("token", [P, T], U32)
        zeros = sb("zeros", [P, MAXT], U32)
        zero_rows = sb("zero_rows", [P, shapes["F"]])
        best = sb("best", [P, 2, T])
        first = sb("first", [P, 2, T])
        hot = [sb(f"hot{k}", [P, T, E]) for k in range(2)]
        work = sb("rwork", [P, T, E])
        rest = sb("rest", [P, T, E])
        probs = sb("rprobs", [P, T, E])
        chosen = sb("chosen", [P, T, E])
        total = sb("total", [P, T])
        zero_r = sb("zero_r", [P, T])
        wk = sb("wk_r", [P, T])
        scan = [sb(f"scan{i}", [P, T, E]) for i in range(2)]
        count_i = sb("count_i", [P, E], I32)
        tiles_f = sb("tiles_f", [P, E])
        tscan = [sb(f"tscan{i}", [P, E]) for i in range(2)]
        start_f = sb("start_f", [P, E])
        slot_f = sb("slot_f", [P, T])
        slot_i = sb("slot_i", [P, T], I32)
        row_i = sb("row_i", [P, T], I32)
        col_i = sb("col_i", [P, T], I32)
        row_f = sb("row_f", [P, T])
        col_f = sb("col_f", [P, T])
        addr = sb("addr", [P, 2, T], U32)
        addr_now = sb("addr_now", [P, 4, 2], U32)
        tok_now = sb("tok_now", [P, 4], U32)
        before_ps = ctx.enter_context(nc.psum_tensor("before_ps", [P, T * E], F32))
        total_ps = ctx.enter_context(nc.psum_tensor("total_ps", [P, T * E], F32))

        loaded = sem("r_loaded")
        cleared = sem("r_cleared")
        step = sem("r_step")
        centred = sem("r_centred")
        exped = sem("r_exped")
        tanhed = sem("r_tanhed")
        chosen_done = sem("r_chosen")
        counted = sem("r_counted")
        addr_done = sem("r_addr")
        staged = sem("r_staged")
        scattered = [sem(f"r_scattered{i}") for i in range(4)]
        table_in = sem("r_table_in")
        y_cleared = sem("r_y_cleared")

        block = ctx.enter_context(nc.Block())

        @block.sync
        def _(sp):
            for dst, src in ((iota_m[:], dram["iota_m"]), (scale_e[:], dram["expert_scale"]),
                             (gates[:], dram["gates"]), (tri[:], dram["tri"]), (token[:], dram["token"])):
                sp.dma_start(dst, src).then_inc(loaded, 16)
            sp.wait_ge(cleared, 3)
            sp.dma_start(dram["slot_table"], zeros[:]).then_inc(table_in, 16)
            sp.wait_ge(table_in, 16)
            with sp.Fori(TOP_K * T, MAXT) as g:
                sp.dma_start(dram["y"][bass.ds(g, 1), :, :].rearrange("g p n -> p (g n)"), zero_rows[:]
                             ).then_inc(y_cleared, 16)
            sp.wait_ge(y_cleared, (MAXT - TOP_K * T) * 16)
            for i in range(4):
                sp.wait_ge(scattered[i], (T // 4) * 2 * 16)
            sp.dma_start(keep["token_of"][:], dram["slot_table"]).then_inc(table_in, 16)
            sp.wait_ge(table_in, 32)

        @block.scalar
        def _(act):
            act.wait_ge(loaded, 16 * 5)
            act.activation(gate_t[:], gates[:, 1:2], ACT.Tanh).then_inc(tanhed, 1)
            act.wait_ge(centred, 1)
            act.activation(probs[:], probs[:], ACT.Exp).then_inc(exped, 1)

        @block.gpsimd
        def _(pool):
            pool.memset(zeros[:], 0).then_inc(cleared, 1)
            pool.memset(ones[:], 1.0).then_inc(cleared, 1)
            pool.memset(zero_rows[:], 0.0).then_inc(cleared, 1)
            pool.wait_ge(addr_done, 2)
            pool.wait_ge(table_in, 16)
            pool.wait_ge(loaded, 16 * 5)
            with pool.Fori(0, T // 4) as q:
                for i in range(4):
                    t = q * 4 + i
                    pool.wait_ge(scattered[i], q * 32)
                    for k in range(2):
                        pool.tensor_copy(addr_now[:, i, k:k + 1], addr[:, k, bass.ds(t, 1)]).then_inc(staged, 1)
                    pool.tensor_copy(tok_now[:, i:i + 1], token[:, bass.ds(t, 1)]).then_inc(staged, 1)
                    pool.wait_ge(staged, q * 12 + 3 * i + 3)
                    for k in range(2):
                        keep["alone"](pool)
                        pool.indirect_dma_start(
                            dram["slot_table"].rearrange("p (m o) -> (p m) o", o=1),
                            bass.IndirectOffsetOnAxis(ap=addr_now[:, i, k:k + 1], axis=0),
                            tok_now[:, i:i + 1], None).then_inc(scattered[i], 16)

        @block.tensor
        def _(pe):
            pe.wait_ge(chosen_done, 1)
            pe.wait_ge(loaded, 16 * 5)
            pe.wait_ge(cleared, 3)
            flat = chosen[:].rearrange("p t e -> p (t e)")
            pe.matmul(before_ps[:], tri[:], flat, start=True, stop=True)
            pe.matmul(total_ps[:], ones[:], flat, start=True, stop=True).then_inc(counted, 1)

        @block.vector
        def _(dve):
            n = [0]

            def link(ins):
                n[0] += 1
                ins.then_inc(step, 1)
                dve.wait_ge(step, n[0])

            def over_e(ap):
                return ap.unsqueeze(2).to_broadcast([P, T, E])

            def over_t(ap):
                return ap.unsqueeze(1).to_broadcast([P, T, E])

            dve.wait_ge(loaded, 16 * 5)
            source = logits[:]
            for k in range(TOP_K):
                link(dve.reduce_max(best[:, k, :], source, axis=AX.X))
                link(dve.tensor_tensor(work[:], source, over_e(best[:, k, :]), ALU.is_equal))
                link(dve.tensor_tensor(work[:], work[:], over_t(iota_m[:]), ALU.mult))
                link(dve.tensor_reduce(first[:, k, :], work[:], axis=AX.X, op=ALU.min))
                link(dve.tensor_tensor(hot[k][:], over_e(first[:, k, :]), over_t(iota_m[:]), ALU.is_equal))
                if k == 0:
                    link(dve.scalar_tensor_tensor(out=rest[:], in0=hot[0][:], scalar=-1e30, in1=logits[:],
                                                  op0=ALU.mult, op1=ALU.add))
                    source = rest[:]
            link(dve.tensor_tensor(chosen[:], hot[0][:], hot[1][:], ALU.add))
            dve.sem_inc(chosen_done, 1)
            dve.tensor_tensor(probs[:], logits[:], over_e(best[:, 0, :]), ALU.subtract).then_inc(centred, 1)
            dve.wait_ge(exped, 1)
            link(dve.reduce_sum(total[:], probs[:], axis=AX.X))
            link(dve.reciprocal(total[:], total[:]))
            link(dve.tensor_tensor(probs[:], probs[:], over_e(total[:]), ALU.mult))
            link(dve.tensor_tensor(work[:], probs[:], chosen[:], ALU.mult))
            link(dve.reduce_sum(total[:], work[:], axis=AX.X))
            link(dve.tensor_scalar(zero_r[:], total[:], 0.0, None, ALU.is_le))
            link(dve.tensor_tensor(total[:], total[:], zero_r[:], ALU.add))
            link(dve.reciprocal(total[:], total[:]))
            dve.wait_ge(tanhed, 1)
            for k in range(TOP_K):
                link(dve.tensor_tensor(work[:], probs[:], hot[k][:], ALU.mult))
                link(dve.reduce_sum(wk[:], work[:], axis=AX.X))
                link(dve.tensor_tensor(wk[:], wk[:], total[:], ALU.mult))
                link(dve.tensor_tensor(work[:], hot[k][:], over_t(scale_e[:]), ALU.mult))
                link(dve.reduce_sum(zero_r[:], work[:], axis=AX.X))
                link(dve.tensor_scalar(wk[:], wk[:], gate_t[:, 0:1], None, ALU.mult))
                link(dve.tensor_tensor(keep["coef"][:, k, :], wk[:], zero_r[:], ALU.mult))
            dve.wait_ge(counted, 1)
            tot = total_ps[:].rearrange("p (t e) -> p t e", e=E)
            link(dve.tensor_copy(scan[0][:], tot))
            cur, s = 0, 1
            while s < T:
                link(dve.tensor_copy(scan[1 - cur][:, 0:s, :], scan[cur][:, 0:s, :]))
                link(dve.tensor_tensor(scan[1 - cur][:, s:T, :], scan[cur][:, s:T, :], scan[cur][:, 0:T - s, :],
                                       ALU.add))
                cur, s = 1 - cur, 2 * s
            link(dve.tensor_scalar(count_i[:], scan[cur][:, T - 1, :], float(P - 1), None, ALU.add))
            link(dve.tensor_scalar(count_i[:], count_i[:], 7, None, ALU.arith_shift_right))
            link(dve.tensor_copy(tiles_f[:], count_i[:]))
            link(dve.tensor_scalar(tiles_f[:], tiles_f[:], 1.0, None, ALU.max))
            link(dve.tensor_copy(tscan[0][:], tiles_f[:]))
            tc, s = 0, 1
            while s < E:
                link(dve.tensor_copy(tscan[1 - tc][:, 0:s], tscan[tc][:, 0:s]))
                link(dve.tensor_tensor(tscan[1 - tc][:, s:E], tscan[tc][:, s:E], tscan[tc][:, 0:E - s], ALU.add))
                tc, s = 1 - tc, 2 * s
            link(dve.tensor_tensor(start_f[:], tscan[tc][:], tiles_f[:], ALU.subtract))
            link(dve.tensor_copy(keep["plan"][:, 0, :], tiles_f[:]))
            link(dve.tensor_copy(keep["plan"][:, 1, :], start_f[:]))
            link(dve.tensor_copy(keep["plan"][:, 2, :], tscan[tc][:]))
            link(dve.tensor_scalar(start_f[:], start_f[:], float(P), None, ALU.mult))
            link(dve.tensor_tensor(rest[:], scan[cur][:], tot, ALU.subtract))
            link(dve.tensor_tensor(rest[:], rest[:], before_ps[:].rearrange("p (t e) -> p t e", e=E), ALU.add))
            link(dve.tensor_tensor(rest[:], rest[:], over_t(start_f[:]), ALU.add))
            for k in range(TOP_K):
                link(dve.tensor_tensor(work[:], rest[:], hot[k][:], ALU.mult))
                link(dve.reduce_sum(slot_f[:], work[:], axis=AX.X))
                link(dve.tensor_copy(slot_i[:], slot_f[:]))
                link(dve.tensor_copy(keep["slot"][:, k, :], slot_f[:]))
                link(dve.tensor_scalar(row_i[:], slot_i[:], P - 1, None, ALU.bitwise_and))
                link(dve.tensor_scalar(col_i[:], slot_i[:], 7, None, ALU.arith_shift_right))
                link(dve.tensor_copy(row_f[:], row_i[:]))
                link(dve.tensor_copy(col_f[:], col_i[:]))
                link(dve.scalar_tensor_tensor(out=slot_f[:], in0=row_f[:], scalar=float(MAXT), in1=col_f[:],
                                              op0=ALU.mult, op1=ALU.add))
                link(dve.tensor_copy(addr[:, k, :], slot_f[:]))
                dve.sem_inc(addr_done, 1)


def expert_phase(nc, keep, dram, shapes):
    E, F, HID, MAXT = shapes["E"], shapes["F"], shapes["HID"], shapes["MAXT"]
    KF, KH = F // P, HID // P
    NH = HID // HALF
    assert NH == 2 and F == 2 * HALF
    up_scale = 1.0 / (S_X * S_E)
    with ExitStack() as ctx:
        def sb(name, shape, dt=F32):
            return ctx.enter_context(nc.sbuf_tensor(name, shape, dt))

        def sem(name):
            return ctx.enter_context(nc.semaphore(name))

        w_up = [sb(f"w_up{i}", [P, KF, 2, NH, 2, HALF], F16) for i in range(2)]
        w_down = sb("w_down", [P, KH, NH, 2, HALF], F16)
        x_rows = sb("x_rows", [P, F])
        idx_now = sb("idx_now", [P, 1], U32)
        xT_hi = sb("xT_hi", [P, KF, P], F16)
        xT_lo = sb("xT_lo", [P, KF, P], F16)
        gelu = sb("gelu", [P, 2, HALF])
        hid = sb("hid", [P, 2, HALF])
        hT_hi = sb("hT_hi", [P, KH, P], F16)
        hT_lo = sb("hT_lo", [P, KH, P], F16)
        y_rows = sb("y_rows", [P, 2, HALF])
        ident = keep["ident"]
        plan = keep["plan"]
        up_ps = [[ctx.enter_context(nc.psum_tensor(f"up_ps{h}{s}", [P, HALF], F32)) for s in range(2)]
                 for h in range(2)]
        tr_ps = [ctx.enter_context(nc.psum_tensor(f"tr_ps{i}", [P, HALF], F32)) for i in range(2)]
        down_ps = [ctx.enter_context(nc.psum_tensor(f"down_ps{i}", [P, HALF], F32)) for i in range(2)]

        up_loaded = [sem(f"up_loaded{i}") for i in range(2)]
        down_loaded = sem("down_loaded")
        idx_done = sem("idx_done")
        x_in = sem("x_in")
        xT_full = sem("e_xT_full")
        xT_hi_done = sem("xT_hi_done")
        xT_lo_done = sem("xT_lo_done")
        up_full = sem("up_full")
        gelu_done = sem("gelu_done")
        hid_done = sem("hid_done")
        hT_full = sem("hT_full")
        hT_hi_done = sem("hT_hi_done")
        hT_lo_done = sem("hT_lo_done")
        down_full = sem("down_full")
        y_done = sem("y_done")
        y_stored = sem("y_stored")

        block = ctx.enter_context(nc.Block())
        n_tiles_ap = plan[0:1, 2, E - 1:E]

        @block.sync
        def _(sp):
            def load_up(e, i):
                src = dram["w_split"][bass.ds(e * (6 * KF), 4 * KF), :, :, :].rearrange("c p l n -> p c l n")
                sp.dma_start(w_up[i][:].rearrange("p k s h l n -> p (k s h) l n"), src).then_inc(up_loaded[i], 16)

            def load_down(e):
                src = dram["w_split"][bass.ds(e * (6 * KF) + 4 * KF, 2 * KH), :, :, :].rearrange("c p l n -> p c l n")
                sp.dma_start(w_down[:].rearrange("p k h l n -> p (k h) l n"), src).then_inc(down_loaded, 16)

            load_up(0, 0)
            load_down(0)
            with sp.Fori(0, E // 2) as e2:
                for i in range(2):
                    e = e2 * 2 + i
                    start = sp.value_load(plan[0:1, 1, bass.ds(e, 1)], min_val=0, max_val=MAXT)
                    tiles = sp.value_load(plan[0:1, 0, bass.ds(e, 1)], min_val=1, max_val=MAXT)
                    nxt = e + 1 if i == 0 else (e + 1) % E
                    sp.wait_ge(up_full, start * 2)
                    load_up(nxt, 1 - i)
                    sp.wait_ge(down_full, (start + tiles) * 2)
                    load_down(nxt)
            for s, n in ((up_loaded[0], E // 2 + 1), (up_loaded[1], E // 2), (down_loaded, E + 1)):
                sp.wait_ge(s, 16 * n)

        @block.gpsimd
        def _(pool):
            n_tiles = pool.value_load(n_tiles_ap, min_val=1, max_val=MAXT - 1)
            with pool.Fori(0, n_tiles + 1) as g:
                pool.wait_ge(x_in, g * 16)
                pool.tensor_copy(idx_now[:], keep["token_of"][:, bass.ds(g, 1)]).then_inc(idx_done, 1)
                pool.wait_ge(idx_done, g + 1)
                pool.wait_ge(xT_full, g * 2)
                keep["alone"](pool)
                pool.indirect_dma_start(x_rows[:], None, dram["xn_rows"],
                                        bass.IndirectOffsetOnAxis(ap=idx_now[:], axis=0)).then_inc(x_in, 16)
            pool.wait_ge(x_in, (n_tiles + 1) * 16)
            keep["alone"](pool)

        @block.scalar
        def _(act):
            n_tiles = act.value_load(n_tiles_ap, min_val=1, max_val=MAXT - 1)

            def x_high(g):
                for half in range(2):
                    act.wait_ge(xT_full, g * 2 + half + 1)
                    act.activation(xT_hi[:, 4 * half:4 * half + 4, :].rearrange("p k t -> p (k t)"),
                                   tr_ps[1 - half][:], ACT.Copy, scale=S_X).then_inc(xT_hi_done, 1)

            def gelu_half(g, h):
                act.wait_ge(up_full, g * 2 + h + 1)
                act.wait_ge(hid_done, g * 2)
                act.activation(gelu[:, h, :], up_ps[h][0][:], ACT.Gelu_apprx_tanh, scale=up_scale
                               ).then_inc(gelu_done, 1)

            def h_high(g, h):
                act.wait_ge(hT_full, g * 2 + h + 1)
                act.activation(hT_hi[:, 4 * h:4 * h + 4, :].rearrange("p k t -> p (k t)"), tr_ps[h][:], ACT.Copy,
                               scale=S_H).then_inc(hT_hi_done, 1)

            def y_out(g):
                for h in range(2):
                    act.wait_ge(down_full, g * 2 + h + 1)
                    if h == 0:
                        act.wait_ge(y_stored, g * 16)
                    act.activation(y_rows[:, h, :], down_ps[h][:], ACT.Copy, scale=1.0 / (S_H * S_E)
                                   ).then_inc(y_done, 1)
                act.wait_ge(y_done, g * 2 + 2)
                act.dma_start(dram["y"][bass.ds(g, 1), :, :].rearrange("g p n -> p (g n)"),
                              y_rows[:].rearrange("p a n -> p (a n)")).then_inc(y_stored, 16)

            x_high(0)
            with act.Fori(0, n_tiles) as g:
                gelu_half(g, 0)
                h_high(g, 0)
                gelu_half(g, 1)
                x_high(g + 1)
                h_high(g, 1)
                y_out(g)
            act.wait_ge(y_stored, n_tiles * 16)
            keep["alone"](act)

        @block.vector
        def _(dve):
            n_tiles = dve.value_load(n_tiles_ap, min_val=1, max_val=MAXT - 1)

            def x_low(g):
                for half in range(2):
                    dve.wait_ge(xT_hi_done, g * 2 + half + 1)
                    dve.scalar_tensor_tensor(out=xT_lo[:, 4 * half:4 * half + 4, :].rearrange("p k t -> p (k t)"),
                                             in0=tr_ps[1 - half][:], scalar=S_X,
                                             in1=xT_hi[:, 4 * half:4 * half + 4, :].rearrange("p k t -> p (k t)"),
                                             op0=ALU.mult, op1=ALU.subtract).then_inc(xT_lo_done, 1)

            def hid_half(g, h):
                dve.wait_ge(gelu_done, g * 2 + h + 1)
                dve.wait_ge(hT_full, g * 2)
                dve.scalar_tensor_tensor(out=hid[:, h, :], in0=up_ps[h][1][:], scalar=up_scale, in1=gelu[:, h, :],
                                         op0=ALU.mult, op1=ALU.mult).then_inc(hid_done, 1)

            def h_low(g, h):
                dve.wait_ge(hT_hi_done, g * 2 + h + 1)
                dve.scalar_tensor_tensor(out=hT_lo[:, 4 * h:4 * h + 4, :].rearrange("p k t -> p (k t)"),
                                         in0=tr_ps[h][:], scalar=S_H,
                                         in1=hT_hi[:, 4 * h:4 * h + 4, :].rearrange("p k t -> p (k t)"),
                                         op0=ALU.mult, op1=ALU.subtract).then_inc(hT_lo_done, 1)

            x_low(0)
            with dve.Fori(0, n_tiles) as g:
                hid_half(g, 0)
                h_low(g, 0)
                hid_half(g, 1)
                x_low(g + 1)
                h_low(g, 1)

        @block.tensor
        def _(pe):
            def transpose_x(g):
                pe.wait_ge(x_in, g * 16 + 16)
                for half in range(2):
                    if half == 0:
                        pe.wait_ge(hT_lo_done, g * 2)
                    for j in range(4):
                        f = (4 * half + j) * P
                        last = pe.transpose(tr_ps[1 - half][:, j * P:(j + 1) * P], x_rows[:, f:f + P], ident[:])
                    last.then_inc(xT_full, 1)

            def up_half(g, h, w, ks):
                for k in ks:
                    for s in range(2):
                        hi, lo = w[:, k, s, h, 0, :], w[:, k, s, h, 1, :]
                        out = up_ps[h][s]
                        pe.matmul(out[:], xT_hi[:, k, :], hi, start=(k == 0), stop=False)
                        pe.matmul(out[:], xT_hi[:, k, :], lo, start=False, stop=False)
                        last = pe.matmul(out[:], xT_lo[:, k, :], hi, start=False, stop=(k == KF - 1))
                return last

            def transpose_h(g, h):
                pe.wait_ge(hid_done, g * 2 + h + 1)
                for j in range(4):
                    last = pe.transpose(tr_ps[h][:, j * P:(j + 1) * P], hid[:, h, j * P:(j + 1) * P], ident[:])
                last.then_inc(hT_full, 1)

            def down(g, ks):
                for k in ks:
                    for h in range(2):
                        hi, lo = w_down[:, k, h, 0, :], w_down[:, k, h, 1, :]
                        pe.matmul(down_ps[h][:], hT_hi[:, k, :], hi, start=(k == 0), stop=False)
                        pe.matmul(down_ps[h][:], hT_hi[:, k, :], lo, start=False, stop=False)
                        last = pe.matmul(down_ps[h][:], hT_lo[:, k, :], hi, start=False, stop=(k == KH - 1))
                        if k == KH - 1:
                            last.then_inc(down_full, 1)

            def tile(g, w):
                pe.wait_ge(xT_lo_done, g * 2 + 2)
                up_half(g, 0, w, range(KF)).then_inc(up_full, 1)
                up_half(g, 1, w, range(KF // 2))
                transpose_h(g, 0)
                up_half(g, 1, w, range(KF // 2, KF)).then_inc(up_full, 1)
                pe.wait_ge(hT_lo_done, g * 2 + 1)
                pe.wait_ge(y_done, g * 2)
                next_x(g)

            def next_x(g):
                pe.wait_ge(x_in, (g + 1) * 16 + 16)
                for half in range(2):
                    for j in range(4):
                        f = (4 * half + j) * P
                        last = pe.transpose(tr_ps[1 - half][:, j * P:(j + 1) * P], x_rows[:, f:f + P], ident[:])
                    last.then_inc(xT_full, 1)

            def tile_down(g, e):
                pe.wait_ge(down_loaded, (e + 1) * 16)
                down(g, range(2))
                pe.wait_ge(xT_lo_done, (g + 1) * 2 + 1)
                transpose_h(g, 1)
                down(g, range(2, KH // 2))
                pe.wait_ge(hT_lo_done, g * 2 + 2)
                down(g, range(KH // 2, KH))

            transpose_x(0)
            with pe.Fori(0, E // 2) as e2:
                for i in range(2):
                    e = e2 * 2 + i
                    start = pe.value_load(plan[0:1, 1, bass.ds(e, 1)], min_val=0, max_val=MAXT)
                    tiles = pe.value_load(plan[0:1, 0, bass.ds(e, 1)], min_val=1, max_val=MAXT)
                    pe.wait_ge(up_loaded[i], (e2 + 1) * 16)
                    keep["alone"](pe)
                    with pe.Fori(0, tiles) as t:
                        g = start + t
                        tile(g, w_up[i])
                        tile_down(g, e)


def combine_phase(nc, keep, dram, shapes):
    T, F, MAXT = shapes["T"], shapes["F"], shapes["MAXT"]
    R = 4
    with ExitStack() as ctx:
        def sb(name, shape, dt=F32):
            return ctx.enter_context(nc.sbuf_tensor(name, shape, dt))

        def sem(name):
            return ctx.enter_context(nc.semaphore(name))

        x1 = sb("x1_rows", [P, R, F])
        y = [sb(f"y{k}_rows", [P, R, F]) for k in range(2)]
        idx = sb("idx_y", [P, R, 2], U32)
        idx_done = sem("c_idx")
        x1_in = [sem(f"c_x1_in{i}") for i in range(R)]
        y_in = [sem(f"c_y_in{i}") for i in range(R)]
        added = sem("c_added")
        stored = [sem(f"c_stored{i}") for i in range(R)]
        block = ctx.enter_context(nc.Block())
        y_rows = dram["y"].rearrange("g p n -> (g p) n")

        @block.sync
        def _(sp):
            with sp.Fori(0, T // R) as q:
                for i in range(R):
                    sp.wait_ge(stored[i], q * 16)
                    sp.dma_start(x1[:, i, :], dram["x1_rows"][bass.ds(q * R + i, 1), :, :]
                                 .rearrange("t p n -> p (t n)")).then_inc(x1_in[i], 16)

        @block.gpsimd
        def _(pool):
            with pool.Fori(0, T // R) as q:
                for i in range(R):
                    pool.wait_ge(y_in[i], q * 32)
                    for k in range(2):
                        pool.tensor_copy(idx[:, i, k:k + 1], keep["slot"][:, k, bass.ds(q * R + i, 1)]
                                         ).then_inc(idx_done, 1)
                    pool.wait_ge(idx_done, q * 2 * R + 2 * i + 2)
                    pool.wait_ge(added, q * 2 * R)
                    for k in range(2):
                        keep["alone"](pool)
                        pool.indirect_dma_start(y[k][:, i, :], None, y_rows,
                                                bass.IndirectOffsetOnAxis(ap=idx[:, i, k:k + 1], axis=0)
                                                ).then_inc(y_in[i], 16)

        @block.vector
        def _(dve):
            with dve.Fori(0, T // R) as q:
                for i in range(R):
                    dve.wait_ge(x1_in[i], q * 16 + 16)
                    dve.wait_ge(y_in[i], q * 32 + 32)
                    for k in range(2):
                        dve.scalar_tensor_tensor(out=x1[:, i, :], in0=y[k][:, i, :],
                                                 scalar=keep["coef"][:, k, bass.ds(q * R + i, 1)],
                                                 in1=x1[:, i, :], op0=ALU.mult, op1=ALU.add).then_inc(added, 1)
                        dve.wait_ge(added, q * 2 * R + 2 * i + k + 1)

        @block.scalar
        def _(act):
            with act.Fori(0, T // R) as q:
                for i in range(R):
                    act.wait_ge(added, q * 2 * R + 2 * i + 2)
                    act.dma_start(dram["out_rows"][bass.ds(q * R + i, 1), :, :].rearrange("t p n -> p (t n)"),
                                  x1[:, i, :]).then_inc(stored[i], 16)
            for i in range(R):
                act.wait_ge(stored[i], (T // R) * 16)


def program(nc, x, ctx, wq, wk, wv, wm, bias_qk, bias_v, bias_m, gates, sign, cos, sin, router, router_scale,
            w_raw, expert_scale, ident, tri, iota_m, token, out):
    B, C, N = x.shape
    E = expert_scale.shape[1]
    T = B * C // P
    MAXT = TOP_K * T + E + 1
    shapes = dict(B=B, N=N, H=C // HD, E=E, F=N, HID=N, T=T, MAXT=MAXT, CHUNKS=w_raw.shape[0] // 2)
    dram = dict(x=x, ctx=ctx, wq=wq, wk=wk, wv=wv, wm=wm, bias_qk=bias_qk, bias_v=bias_v, bias_m=bias_m, gates=gates,
                sign=sign, cos=cos, sin=sin, router=router, router_scale=router_scale, w_raw=w_raw,
                expert_scale=expert_scale, tri=tri, iota_m=iota_m, token=token)
    dram["shift"] = nc.dram_tensor("shift_scratch", (2, P // HD * (N // P), P), F16).ap()
    dram["recip"] = nc.dram_tensor("recip_scratch", (P, N // HD), F32).ap()
    dram["den"] = nc.dram_tensor("den_scratch", (P // HD, N), F32).ap()
    dram["x1"] = nc.dram_tensor("x1_scratch", (B, C, N), F32).ap()
    dram["xn"] = nc.dram_tensor("xn_scratch", (B, C, N), F32).ap()
    dram["w_split"] = nc.dram_tensor("w_split_scratch", (w_raw.shape[0], P, 2, N // 2), F16).ap()
    dram["w_raw_pieces"] = w_raw.rearrange("c p n -> p c n")
    dram["w_split_pieces"] = dram["w_split"].rearrange("c p l n -> p c (l n)")
    dram["slot_table"] = nc.dram_tensor("slot_table_scratch", (P, MAXT), U32).ap()
    dram["y"] = nc.dram_tensor("y_scratch", (MAXT, P, N), F32).ap()
    dram["xn_rows"] = dram["xn"].rearrange("b c n -> (b c) n")
    dram["x1_rows"] = dram["x1"].rearrange("b (o p) n -> (b o) p n", p=P)
    dram["out_rows"] = out.rearrange("b (o p) n -> (b o) p n", p=P)

    with ExitStack() as ctx_:
        def sb(name, shape, dt=F32):
            return ctx_.enter_context(nc.sbuf_tensor(name, shape, dt))

        keep = dict(ident=sb("ident", [P, P]), logits=sb("logits", [P, T, E]))
        passed = {name: ctx_.enter_context(nc.semaphore(f"passed_{name}")) for name in ("sp", "act", "dve", "pool", "pe")}
        names = {id(nc.sync): "sp", id(nc.scalar): "act", id(nc.vector): "dve", id(nc.gpsimd): "pool",
                 id(nc.tensor): "pe"}

        def alone(eng):
            eng.sem_inc(passed[names[id(eng)]], 1)

        keep["alone"] = alone
        ident_in = ctx_.enter_context(nc.semaphore("ident_in"))
        with nc.Block() as block:
            @block.sync
            def _(sp):
                sp.dma_start(keep["ident"][:], ident).then_inc(ident_in, 16)
                sp.wait_ge(ident_in, 16)
        attention_phase(nc, keep, dram, shapes)
        keep |= dict(token_of=sb("token_of", [P, MAXT], U32), coef=sb("coef", [P, TOP_K, T]),
                     slot=sb("slot", [P, TOP_K, T], U32), plan=sb("plan", [P, 3, E], I32))
        routing_phase(nc, keep, dram, shapes)
        expert_phase(nc, keep, dram, shapes)
        combine_phase(nc, keep, dram, shapes)


def kernel(x, ctx_2048, g_xattn, g_ffn, L0_xattn_encoding, L0_xattn_Wq, L0_xattn_bq, L0_xattn_Wk, L0_xattn_bk,
           L0_xattn_Wv, L0_xattn_bv, L0_xattn_Wm, L0_xattn_bm, L0_ffn_router_logits, L0_ffn_gating_einsum,
           L0_ffn_linear, L0_ffn_per_expert_scale, L0_ffn_router_scale):
    import numpy as np
    import concourse.bacc as bacc
    from concourse.bass_utils import run_bass_kernel_spmd as run

    a = np.ascontiguousarray
    x, ctx = np.asarray(x), np.asarray(ctx_2048)
    B, C, N = x.shape
    H = C // HD
    E = L0_ffn_router_logits.shape[1]
    T = B * C // P

    def by_head(w):
        w = np.asarray(w)
        return w.reshape(HD, H, *w.shape[1:]).swapaxes(0, 1).reshape(w.shape)

    enc = np.asarray(L0_xattn_encoding)
    gating = np.asarray(L0_ffn_gating_einsum)
    linear = np.asarray(L0_ffn_linear)
    up = gating.transpose(0, 3, 1, 2).reshape(E, N // P, P, 2, -1).swapaxes(2, 3).reshape(E, 2 * N // P, P, -1)
    arrays = {
        "x": a(x), "ctx": a(ctx),
        "wq": a(by_head(L0_xattn_Wq).T), "wk": a(by_head(L0_xattn_Wk).T), "wv": a(by_head(L0_xattn_Wv).T),
        "wm": a(by_head(np.asarray(L0_xattn_Wm).T)),
        "bias_qk": a(np.stack([by_head(b).reshape(C // P, P).T for b in (L0_xattn_bq, L0_xattn_bk)], 1)),
        "bias_v": a(np.broadcast_to(by_head(L0_xattn_bv)[None], (P, C))),
        "bias_m": a(np.asarray(L0_xattn_bm).reshape(C // P, P).T),
        "gates": a(np.broadcast_to(np.concatenate([np.asarray(g_xattn), np.asarray(g_ffn)])[None], (P, 2))),
        "sign": np.tile(np.array([-1, 1], np.float32), P // 2).reshape(P, 1),
        "cos": a(np.tile(enc[0, 0, 0].T, (P // HD, 1))), "sin": a(np.tile(enc[1, 0, 0].T, (P // HD, 1))),
        "router": a(np.asarray(L0_ffn_router_logits).reshape(N // P, P, E).swapaxes(0, 1)),
        "router_scale": a(np.asarray(L0_ffn_router_scale).reshape(N // P, P).T),
        "w_raw": a(np.concatenate([up, linear.reshape(E, -1, P, N)], 1)
                   .reshape(-1, P, 2, N // 2).swapaxes(1, 2).reshape(-1, P, N // 2)),
        "expert_scale": a(np.broadcast_to(np.asarray(L0_ffn_per_expert_scale)[None], (P, E))),
        "ident": np.eye(P, dtype=np.float32), "tri": np.triu(np.ones((P, P), np.float32), 1),
        "iota_m": a(np.broadcast_to(np.arange(E, dtype=np.float32) - E, (P, E))),
        "token": a(np.arange(T * P, dtype=np.uint32).reshape(T, P).T),
    }
    nc = bacc.Bacc("TRN2", target_bir_lowering=False, num_devices=1)
    args = [nc.dram_tensor(f"in_{k}", v.shape, mybir.dt.from_np(v.dtype), kind="ExternalInput").ap()
            for k, v in arrays.items()]
    out = nc.dram_tensor("out_0", (B, C, N), F32, kind="ExternalOutput").ap()
    program(nc, *args, out)
    r = run(nc, [{f"in_{k}": v for k, v in arrays.items()}], core_ids=[0])
    return r.results[0]["out_0"]
```
